# Optimizing a Trainium2 kernel written in Bass

```python
import numpy as np
import jax
import jax.numpy as jnp

def _softmax(x, axis=-1):
    return jax.nn.softmax(x, axis=axis)

def _gelu(x):
    return jax.nn.gelu(x, approximate=True)

def _silu(x):
    return jax.nn.silu(x)

def _sigmoid(x):
    return jax.nn.sigmoid(x)

def _layernorm(x, axis=-1, eps=1e-05):
    m = jnp.mean(x, axis=axis, keepdims=True)
    v = jnp.var(x, axis=axis, keepdims=True)
    return (x - m) / jnp.sqrt(v + eps)

def _scatter_add(tgt, idx, src, axis=0):
    return tgt.at[idx].add(src)

def _segment_sum(src, seg, n):
    return jax.ops.segment_sum(src, seg, n)
kernel_name = 'mk_cond_resid_d1_seqx_r2_a332c3'

def setup_inputs(seed: int=0):
    np.random.seed(seed)
    _w = jnp.asarray

    def _rec_inputs():
        import jax
        import jax.numpy as jnp
        _rk = jax.random.key(seed)
        x = -0.000125 + 0.9999 * jax.random.normal(jax.random.fold_in(_rk, 1), (32, 128, 512), jnp.float32)
        _lenS = 128 - jax.random.randint(jax.random.fold_in(_rk, 7), (32,), 0, max(1, 128 // 4) + 1, jnp.int32)
        _lenS2 = 128 - jax.random.randint(jax.random.fold_in(_rk, 8), (32,), 0, max(1, 128 // 4) + 1, jnp.int32)
        cond_1024 = -0.00493535 + 1.00056 * jax.random.normal(jax.random.fold_in(_rk, 11), (32, 512), jnp.float32)
        return (x, cond_1024)
    x, cond_1024 = _rec_inputs()

    def _L0_cond_setup():
        import jax, jax.numpy as jnp
        import numpy as np
        import math
        D = 512
        H = 512
        key = jax.random.key(seed)
        k1, k2, k3, k4 = jax.random.split(key, 4)
        x = jax.random.normal(k1, (64, 256, D), dtype=jnp.float32)
        h0 = jax.random.normal(k2, (64, H), dtype=jnp.float32)
        Wx = jax.random.normal(k3, (D, 4 * H), dtype=jnp.float32) / math.sqrt(D)
        Wh = jax.random.normal(k4, (H, 4 * H), dtype=jnp.float32) / math.sqrt(H)
        b = jnp.zeros((4 * H,), dtype=jnp.float32)
        return {'x': x, 'h0': h0, 'Wx': Wx, 'Wh': Wh, 'b': b}
    _L0_cond_all = _L0_cond_setup()
    _L0_cond_in = {k: v for k, v in _L0_cond_all.items() if k in ('Wx', 'Wh', 'b')}
    del _L0_cond_all
    return {'x': x, 'cond_1024': cond_1024, 'L0_cond_Wx': _L0_cond_in['Wx'], 'L0_cond_Wh': _L0_cond_in['Wh'], 'L0_cond_b': _L0_cond_in['b']}

def reference(x, cond_1024, L0_cond_Wx, L0_cond_Wh, L0_cond_b):
    import jax
    import jax.numpy as jnp

    def _L0_cond_ref(x, h0, Wx, Wh, b):
        import jax, jax.numpy as jnp
        import numpy as np
        import math
        D = 512
        H = 512
        xz = jnp.einsum('ntd,dk->ntk', x, Wx) + b
        c0 = jnp.zeros_like(h0)

        def step(carry, xz_t):
            prev_h, prev_c = carry
            z = xz_t + prev_h @ Wh
            ai, af, ao, ag = jnp.split(z, 4, axis=1)
            i = jax.nn.sigmoid(ai)
            f = jax.nn.sigmoid(af)
            o = jax.nn.sigmoid(ao)
            g = jnp.tanh(ag)
            next_c = f * prev_c + i * g
            next_h = o * jnp.tanh(next_c)
            return ((next_h, next_c), next_h)
        _, hs = jax.lax.scan(step, (h0, c0), jnp.swapaxes(xz, 0, 1))
        return jnp.swapaxes(hs, 0, 1)
    x = x + _L0_cond_ref(x, cond_1024, L0_cond_Wx, L0_cond_Wh, L0_cond_b)
    return x

_drawn_inputs = setup_inputs


def setup_inputs(seed=0):
    import zlib

    import numpy as np

    out = dict(_drawn_inputs(seed))
    spreads = {'L0_cond_b': (0.0, 0.1)}
    factors = {'cond_1024': 3.314}
    for name, (base, spread) in spreads.items():
        noise = np.random.default_rng([zlib.crc32(name.encode()), seed]).standard_normal(out[name].shape)
        drawn = base * np.exp(spread * noise) if base else spread * noise
        out[name] = jnp.asarray(drawn.astype(out[name].dtype))
    for name, factor in factors.items():
        out[name] = (out[name] * factor).astype(out[name].dtype)
    return out
```

```python
import concourse.bass as bass
from concourse import mybir
from contextlib import ExitStack


def lstm_residual_kernel(nc: bass.Bass, xT: bass.AP, xr: bass.AP, h0T: bass.AP, wx: bass.AP, wh: bass.AP,
                         bias: bass.AP, out: bass.AP):
    fp32 = mybir.dt.float32
    ALU = mybir.AluOpType
    ACT = mybir.ActivationFunctionType

    P, T, XC = xT.shape
    KC = 4
    B = XC // KC
    NS = P // B
    HS = xr.shape[2]
    G = 4 * HS
    C = 2
    U = 2 * C
    NI = T // U

    with ExitStack() as ctx:
        def sb(name, shape, dt=fp32):
            return ctx.enter_context(nc.sbuf_tensor(name, shape, dt))

        def sem(name):
            return ctx.enter_context(nc.semaphore(name))

        wx_sb = sb("wx_sb", [P, KC, NS, G])
        wh_sb = sb("wh_sb", [P, KC, NS, G])
        bias_sb = sb("bias_sb", [1, NS, G])
        ones = sb("ones", [1, B])
        x_in = sb("x_in", [P, U, XC])
        res = sb("res", [P, U, HS])
        y = sb("y", [P, U, HS])
        gc = sb("gc", [P, 2 * HS])
        fi = sb("fi", [P, 3 * HS])
        prod = sb("prod", [P, 2 * HS])
        tc_sb = sb("tc_sb", [P, HS])
        h = sb("h", [P, 2, HS])
        hT = sb("hT", [P, HS])
        z = [ctx.enter_context(nc.psum_tensor(f"z{i}", [P, G], fp32)) for i in range(2)]

        w_loaded = sem("w_loaded")
        wh_loaded = sem("wh_loaded")
        small_loaded = sem("small_loaded")
        ones_set = sem("ones_set")
        c_zeroed = sem("c_zeroed")
        x_loaded = [sem(f"x_loaded{i}") for i in range(2)]
        res_loaded = [sem(f"res_loaded{i}") for i in range(2)]
        x_done = sem("x_done")
        z_done = sem("z_done")
        g_ready = sem("g_ready")
        gates_ready = sem("gates_ready")
        prod_ready = sem("prod_ready")
        c_ready = sem("c_ready")
        tanhc_ready = sem("tanhc_ready")
        h_ready = sem("h_ready")
        hT_ready = sem("hT_ready")
        y_ready = sem("y_ready")
        stored = [sem(f"stored{i}") for i in range(2)]

        block = ctx.enter_context(nc.Block())

        @block.sync
        def _(sp):
            sp.dma_start(bias_sb[:, :, :], bias).then_inc(small_loaded, 16)
            sp.dma_start(hT[:, :], h0T).then_inc(small_loaded, 16)

            def load(it, half, first):
                if not first:
                    sp.wait_ge(x_done, it * U - (1 - half) * C)
                    sp.wait_ge(y_ready, it * U - (1 - half) * C)
                s = slice(half * C, half * C + C)
                t0 = it * U + half * C
                sp.dma_start(x_in[:, s, :], xT[:, bass.ds(t0, C), :]).then_inc(x_loaded[half], 16)
                sp.dma_start(res[:, s, :], xr[:, bass.ds(t0, C), :]).then_inc(res_loaded[half], 16)

            def store(it, half):
                s = slice(half * C, half * C + C)
                t0 = it * U + half * C
                sp.wait_ge(y_ready, it * U + half * C + C)
                sp.dma_start(out[:, bass.ds(t0, C), :], y[:, s, :]).then_inc(stored[half], 16)

            load(0, 0, True)
            for kc in range(KC):
                sp.dma_start(wx_sb[:, kc, :, :], wx[:, kc, :, :]).then_inc(w_loaded, 16)
            load(0, 1, True)
            for kc in range(KC):
                sp.dma_start(wh_sb[:, kc, :, :], wh[:, kc, :, :]).then_inc(wh_loaded, 16)
            with sp.Fori(1, NI) as it:
                for half in range(2):
                    load(it, half, False)
                    store(it - 1, half)
            for half in range(2):
                store(NI - 1, half)
            for half in range(2):
                sp.wait_ge(stored[half], 16 * NI)

        @block.tensor
        def _(pe):
            def x_part(it, u, first):
                zt = z[u % 2]
                if u % C == 0:
                    pe.wait_ge(x_loaded[u // C], 16 * it + 16)
                if not first:
                    pe.wait_ge(gates_ready, it * U + u - 1)
                for kc in range(KC):
                    for j in range(NS):
                        mm = pe.matmul(zt[j * B:(j + 1) * B, :], x_in[:, u, kc * B:(kc + 1) * B],
                                       wx_sb[:, kc, j, :], start=(kc == 0), stop=False)
                for j in range(NS):
                    mm = pe.matmul(zt[j * B:(j + 1) * B, :], ones[:, :], bias_sb[:, j, :], start=False, stop=False)
                mm.then_inc(x_done, 1)

            def h_part(it, u, first):
                zt = z[u % 2]
                if not first:
                    pe.wait_ge(hT_ready, it * U + u)
                for kc in range(KC):
                    for j in range(NS):
                        mm = pe.matmul(zt[j * B:(j + 1) * B, :], hT[:, kc * B:(kc + 1) * B],
                                       wh_sb[:, kc, j, :], start=False, stop=(kc == KC - 1))
                mm.then_inc(z_done, 1)

            pe.wait_ge(small_loaded, 32)
            pe.wait_ge(ones_set, 1)
            pe.wait_ge(w_loaded, 16 * KC)
            x_part(0, 0, True)
            pe.wait_ge(wh_loaded, 16 * KC)
            h_part(0, 0, True)
            x_part(0, 1, True)
            for u in range(1, U):
                h_part(0, u, False)
                if u + 1 < U:
                    x_part(0, u + 1, False)
            with pe.Fori(1, NI) as it:
                for u in range(U):
                    x_part(it, u, False)
                    h_part(it, u, False)

        @block.scalar
        def _(act):
            def step(it, u):
                t = it * U + u
                zt = z[u % 2]
                act.wait_ge(z_done, t + 1)
                nc.scalar.activation(gc[:, 0:HS], zt[:, 3 * HS:4 * HS], ACT.Tanh).then_inc(g_ready, 1)
                nc.scalar.activation(fi[:, :], zt[:, 0:3 * HS], ACT.Sigmoid).then_inc(gates_ready, 1)
                act.wait_ge(c_ready, t + 1)
                nc.scalar.activation(tc_sb[:, :], gc[:, HS:2 * HS], ACT.Tanh).then_inc(tanhc_ready, 1)

            with act.Fori(0, NI) as it:
                for u in range(U):
                    step(it, u)

        @block.vector
        def _(dve):
            nc.vector.memset(ones[:, :], 1.0).then_inc(ones_set, 1)
            nc.vector.memset(gc[:, HS:2 * HS], 0.0).then_inc(c_zeroed, 1)
            dve.wait_ge(c_zeroed, 1)

            def step(it, u, first):
                t = it * U + u
                dve.wait_ge(g_ready, t + 1)
                dve.wait_ge(gates_ready, t + 1)
                nc.vector.tensor_tensor(prod[:, :], fi[:, 0:2 * HS], gc[:, :], ALU.mult).then_inc(prod_ready, 1)
                dve.wait_ge(prod_ready, t + 1)
                nc.vector.tensor_tensor(gc[:, HS:2 * HS], prod[:, 0:HS], prod[:, HS:2 * HS],
                                        ALU.add).then_inc(c_ready, 1)
                dve.wait_ge(tanhc_ready, t + 1)
                if not first:
                    dve.wait_ge(y_ready, t - 1)
                nc.vector.tensor_tensor(h[:, u % 2, :], fi[:, 2 * HS:3 * HS], tc_sb[:, :], ALU.mult).then_inc(h_ready, 1)
                dve.wait_ge(h_ready, t + 1)
                dve.wait_ge(z_done, t + 1)
                nc.vector.transpose(hT[:, :], h[:, u % 2, :]).then_inc(hT_ready, 1)

            for u in range(U):
                step(0, u, u < 2)
            with dve.Fori(1, NI) as it:
                for u in range(U):
                    step(it, u, False)

        @block.gpsimd
        def _(pool):
            def step(it, u, first):
                t = it * U + u
                half = u // C
                if u % C == 0:
                    pool.wait_ge(res_loaded[half], 16 * it + 16)
                    if not first:
                        pool.wait_ge(stored[half], 16 * it)
                pool.wait_ge(h_ready, t + 1)
                nc.gpsimd.tensor_tensor(y[:, u, :], h[:, u % 2, :], res[:, u, :], ALU.add).then_inc(y_ready, 1)

            for u in range(U):
                step(0, u, True)
            with pool.Fori(1, NI) as it:
                for u in range(U):
                    step(it, u, False)


def kernel(x, cond_1024, L0_cond_Wx, L0_cond_Wh, L0_cond_b):
    import numpy as np
    import concourse.bacc as bacc
    from concourse import mybir as mb
    from concourse.bass_utils import run_bass_kernel_spmd

    x = np.asarray(x)
    B, T, D = x.shape
    NS, HS, KC, P = 4, 128, 4, 128
    wx = np.asarray(L0_cond_Wx).reshape(KC, P, 4, NS, HS).transpose(1, 0, 3, 2, 4)
    wh = np.asarray(L0_cond_Wh).reshape(NS, 4, 32, 4, NS, HS).transpose(0, 2, 1, 4, 3, 5)
    h0 = np.asarray(cond_1024).reshape(B, NS, 4, 32).transpose(1, 3, 2, 0)
    arrays = {
        "xT": x.reshape(B, T, KC, P).transpose(3, 1, 2, 0).reshape(P, T, KC * B),
        "xr": x.reshape(B, T, NS, HS).transpose(2, 0, 1, 3).reshape(P, T, HS),
        "h0T": h0.reshape(P, KC * B),
        "wx": wx.reshape(P, KC, NS, 4 * HS),
        "wh": wh.reshape(P, KC, NS, 4 * HS),
        "bias": np.asarray(L0_cond_b).reshape(1, 4, NS, HS).transpose(0, 2, 1, 3).reshape(1, NS, 4 * HS),
    }
    arrays = {f"in_{k}": np.ascontiguousarray(v) for k, v in arrays.items()}
    nc = bacc.Bacc("TRN2", target_bir_lowering=False, num_devices=1)
    args = [nc.dram_tensor(k, v.shape, mb.dt.from_np(v.dtype), kind="ExternalInput").ap() for k, v in arrays.items()]
    args.append(nc.dram_tensor("out_y", (P, T, HS), mb.dt.float32, kind="ExternalOutput").ap())
    lstm_residual_kernel(nc, *args)
    r = run_bass_kernel_spmd(nc, [arrays], core_ids=[0])
    y = np.asarray(r.results[0]["out_y"])
    return y.reshape(NS, B, T, HS).transpose(1, 2, 0, 3).reshape(B, T, NS * HS)
```

```python
import concourse.bass as bass
from concourse import mybir
from contextlib import ExitStack


def lstm_residual_kernel(nc: bass.Bass, xT: bass.AP, xr: bass.AP, h0T: bass.AP, wx: bass.AP, wh: bass.AP,
                         bias: bass.AP, out: bass.AP):
    fp32 = mybir.dt.float32
    fp16 = mybir.dt.float16
    i32 = mybir.dt.int32
    ALU = mybir.AluOpType
    ACT = mybir.ActivationFunctionType
    AX = mybir.AxisListType
    RMAX = bass.bass_isa.ReduceOp.max

    P, T, XC = xT.shape
    NS, G = bias.shape
    B = P // NS
    KC = XC // B
    HS = G // 4
    C = 2
    U = 2 * C
    NI = T // U
    W = NS * G
    XM = 8
    NX = T // XM
    PIECE = 1024
    NP = KC * W // PIECE
    TINY = 2.0 ** -48
    EXPONENT = 0x7F800000

    with ExitStack() as ctx:
        def sb(name, shape, dt=fp32):
            return ctx.enter_context(nc.sbuf_tensor(name, shape, dt))

        def sem(name):
            return ctx.enter_context(nc.semaphore(name))

        w32 = [sb(f"w{n}_32", [P, KC * W]) for n in "xh"]
        w_hi = [sb(f"w{n}_hi", [P, KC * W], fp16) for n in "xh"]
        w_lo = [sb(f"w{n}_lo", [P, KC * W], fp16) for n in "xh"]
        x_all = sb("x_all", [P, T * XC])
        x_hi = sb("x_hi", [P, U * XC], fp16)
        x_lo = sb("x_lo", [P, U * XC], fp16)
        zeros = x_hi
        bias_raw = sb("bias_raw", [P, G])
        res = sb("res", [P, U, HS])
        y = sb("y", [P, U, HS])
        gc = sb("gc", [P, 2 * HS])
        ifo = sb("ifo", [P, 3 * HS])
        prod = sb("prod", [P, 2 * HS])
        tanhc = sb("tanhc", [P, HS])
        h = sb("h", [P, HS])
        hT = sb("hT", [P, KC * B])
        hT_hi = sb("hT_hi", [P, KC * B], fp16)
        hT_lo = sb("hT_lo", [P, KC * B], fp16)
        magn = [sb(f"magn_{n}", [P, k]) for n, k in (("wx", KC), ("wh", KC), ("x", NX))]
        most = sb("most", [P, 3])
        most_all = sb("most_all", [P, 3])
        pow2 = sb("pow2", [P, 3])
        scl = sb("scl", [P, 12])
        w_scaled = sb("w_scaled", [P, PIECE // 2])
        warm = sb("warm", [P, 1])
        z = [ctx.enter_context(nc.psum_tensor(f"z{i}", [P, G], fp32)) for i in range(2)]

        w_scale = [scl[:, 0:1], scl[:, 1:2]]
        s_x, s_h, s_both = scl[:, 2:3], scl[:, 3:4], scl[:, 4:5]
        x_scale, h_scale, z_unscale, h_unscale = scl[:, 5:6], scl[:, 6:7], scl[:, 7:8], scl[:, 8:9]
        inv_w = [scl[:, 9:10], scl[:, 10:11]]
        inv_x = scl[:, 11:12]

        h0_loaded = sem("h0_loaded")
        bias_loaded = sem("bias_loaded")
        w_loaded = [[sem(f"w{n}_loaded{kc}") for kc in range(KC)] for n in "xh"]
        x_loaded = [sem(f"x_loaded{n}") for n in range(NX)]
        res_loaded = [sem(f"res_loaded{i}") for i in range(2)]
        stored = [sem(f"stored{i}") for i in range(2)]
        zeros_set = sem("zeros_set")
        c_zeroed = sem("c_zeroed")
        opened = sem("opened")
        seeded = sem("seeded")
        x_done = sem("x_done")
        z_done = sem("z_done")
        g_ready = sem("g_ready")
        gates_ready = sem("gates_ready")
        prod_ready = sem("prod_ready")
        c_ready = sem("c_ready")
        tanhc_ready = sem("tanhc_ready")
        h_ready = sem("h_ready")
        hT_ready = sem("hT_ready")
        hi_ready = sem("hi_ready")
        lo_ready = sem("lo_ready")
        y_ready = sem("y_ready")
        xs_hi = sem("xs_hi")
        xs_lo = sem("xs_lo")
        magn_ready = sem("magn_ready")
        most_ready = sem("most_ready")
        all_ready = sem("all_ready")
        scalar_done = sem("scalar_done")
        w_scale_ready = sem("w_scale_ready")
        scales_ready = sem("scales_ready")
        w_hi_ready = [sem("wx_hi_ready"), sem("wh_hi_ready")]
        w_lo_ready = [sem("wx_lo_ready"), sem("wh_lo_ready")]
        w_scaled_ready = sem("w_scaled_ready")

        block = ctx.enter_context(nc.Block())

        @block.sync
        def _(sp):
            def load_x(n):
                sp.dma_start(x_all[:, n * XM * XC:(n + 1) * XM * XC],
                             xT[:, n * XM:(n + 1) * XM, :]).then_inc(x_loaded[n], 16)

            def load_res(it, half, first):
                if not first:
                    sp.wait_ge(y_ready, it * U - (1 - half) * C)
                sp.dma_start(res[:, half * C:half * C + C, :],
                             xr[:, bass.ds(it * U + half * C, C), :]).then_inc(res_loaded[half], 16)

            def store(it, half):
                sp.wait_ge(y_ready, it * U + half * C + C)
                sp.dma_start(out[:, bass.ds(it * U + half * C, C), :],
                             y[:, half * C:half * C + C, :]).then_inc(stored[half], 16)

            load_x(0)
            for n in range(2):
                for kc in range(KC):
                    sp.dma_start(w32[n][:, kc * W:(kc + 1) * W], (wx, wh)[n][:, kc, :]).then_inc(w_loaded[n][kc], 16)
            for half in range(2):
                load_res(0, half, True)
            for n in range(1, NX):
                load_x(n)
            with sp.Fori(1, NI) as it:
                for half in range(2):
                    load_res(it, half, False)
                    store(it - 1, half)
            for half in range(2):
                store(NI - 1, half)
            for half in range(2):
                sp.wait_ge(stored[half], 16 * NI)

        @block.tensor
        def _(pe):
            def product(u, stationary, moving, cols, last):
                for kc in range(KC):
                    for j in range(NS):
                        mm = pe.matmul(z[u % 2][j * B:(j + 1) * B, :], stationary[:, cols + kc * B:cols + (kc + 1) * B],
                                       moving[:, kc * W + j * G:kc * W + (j + 1) * G], start=False,
                                       stop=last and kc == KC - 1, skip_group_check=True)
                return mm

            def x_part32(u):
                pe.wait_ge(seeded, u + 1)
                product(u, x_all, w32[0], u * XC, False).then_inc(x_done, 1)

            def h_part32(u):
                if u > 0:
                    pe.wait_ge(hT_ready, u)
                product(u, hT, w32[1], 0, True).then_inc(z_done, 1)

            def x_part(it, u):
                t = it * U + u
                pe.wait_ge(seeded, t + 1)
                if u % C == 0:
                    pe.wait_ge(xs_lo, it * (U // C) + u // C - 1)
                product(u, x_hi, w_hi[0], u * XC, False)
                product(u, x_hi, w_lo[0], u * XC, False)
                product(u, x_lo, w_hi[0], u * XC, False).then_inc(x_done, 1)

            def h_part(it, u):
                t = it * U + u
                pe.wait_ge(hi_ready, t - U + 1)
                product(u, hT_hi, w_hi[1], 0, False)
                product(u, hT_hi, w_lo[1], 0, False)
                pe.wait_ge(lo_ready, t - U + 1)
                product(u, hT_lo, w_hi[1], 0, True).then_inc(z_done, 1)

            pe.wait_ge(zeros_set, 1)
            for i in range(2):
                for j in range(NS):
                    mm = pe.matmul(z[i][j * B:(j + 1) * B, :], zeros[:, 0:B], zeros[:, :], start=True, stop=True)
                mm.then_inc(opened, 1)

            pe.wait_ge(x_loaded[0], 16)
            for kc in range(KC):
                pe.wait_ge(w_loaded[0][kc], 16)
            x_part32(0)
            pe.wait_ge(h0_loaded, 16)
            for kc in range(KC):
                pe.wait_ge(w_loaded[1][kc], 16)
            h_part32(0)
            for u in range(1, U):
                x_part32(u)
                h_part32(u)
            for n in range(2):
                pe.wait_ge(w_hi_ready[n], NP)
                pe.wait_ge(w_lo_ready[n], (NP, 2 * NP)[n])
            with pe.Fori(1, NI) as it:
                for u in range(U):
                    x_part(it, u)
                    h_part(it, u)

        @block.scalar
        def _(act):
            act.dma_start(hT[:, :], h0T).then_inc(h0_loaded, 16)
            for j in range(NS):
                act.dma_start(bias_raw[j * B:(j + 1) * B, :], bias[j, :].partition_broadcast(B)).then_inc(bias_loaded, 16)
            act.wait_ge(zeros_set, 1)
            nc.scalar.activation(warm[:, :], zeros[:, 0:1], ACT.Sigmoid)
            act.wait_ge(bias_loaded, 16 * NS)
            act.wait_ge(opened, 2)
            for i in range(2):
                nc.scalar.activation(z[i][:, :], bias_raw[:, :], ACT.Copy).then_inc(seeded, 1)

            def gates(t, u, unscale):
                act.wait_ge(z_done, t + 1)
                nc.scalar.activation(gc[:, 0:HS], z[u % 2][:, 3 * HS:4 * HS], ACT.Tanh,
                                     scale=unscale).then_inc(g_ready, 1)
                nc.scalar.activation(ifo[:, :], z[u % 2][:, 0:3 * HS], ACT.Sigmoid,
                                     scale=unscale).then_inc(gates_ready, 1)
                act.wait_ge(c_ready, t + 1)
                nc.scalar.activation(tanhc[:, :], gc[:, HS:2 * HS], ACT.Tanh).then_inc(tanhc_ready, 1)

            def seed(u, scale):
                nc.scalar.activation(z[u % 2][:, :], bias_raw[:, :], ACT.Copy, scale=scale).then_inc(seeded, 1)

            def split_hi(n, first, count):
                for p in range(first, first + count):
                    s = slice(p * PIECE, (p + 1) * PIECE)
                    nc.scalar.activation(w_hi[n][:, s], w32[n][:, s], ACT.Copy,
                                         scale=w_scale[n]).then_inc(w_hi_ready[n], 1)

            act.wait_ge(w_scale_ready, 1)
            split_hi(0, 0, NP)
            act.wait_ge(w_scale_ready, 2)
            for u in range(U):
                gates(u, u, 1.0)
                if u == 2:
                    act.wait_ge(scales_ready, 1)
                act.wait_ge(gates_ready, u + 1)
                seed(u, 1.0 if u + 2 < U else s_both)
                if u < 3:
                    split_hi(1, 3 * u, min(3, NP - 3 * u))
            with act.Fori(1, NI) as it:
                for u in range(U):
                    t = it * U + u
                    gates(t, u, z_unscale)
                    act.wait_ge(gates_ready, t + 1)
                    seed(u, s_both)

        @block.vector
        def _(dve):
            nc.vector.memset(zeros[:, :], 0.0).then_inc(zeros_set, 1)
            nc.vector.memset(gc[:, HS:2 * HS], 0.0).then_inc(c_zeroed, 1)
            dve.wait_ge(c_zeroed, 1)
            count = [0]

            def link(ins):
                count[0] += 1
                ins.then_inc(scalar_done, 1)
                dve.wait_ge(scalar_done, count[0])

            def magnitude(n, piece, src):
                nc.vector.tensor_reduce(magn[n][:, piece:piece + 1], src, AX.X, ALU.max,
                                        apply_absolute_value=True).then_inc(magn_ready, 1)

            def w_magnitudes(n):
                for kc in range(KC):
                    dve.wait_ge(w_loaded[n][kc], 16)
                    magnitude(n, kc, w32[n][:, kc * W:(kc + 1) * W])
                dve.wait_ge(magn_ready, KC * (n + 1))
                nc.vector.tensor_reduce(most[:, n:n + 1], magn[n][:, :], AX.X, ALU.max).then_inc(most_ready, 1)

            def power(n):
                dve.wait_ge(all_ready, n + 1)
                link(nc.vector.tensor_scalar(pow2[:, n:n + 1], most_all[:, n:n + 1], TINY, None, ALU.max))
                link(nc.vector.tensor_scalar(pow2[:, n:n + 1].bitcast(i32), pow2[:, n:n + 1].bitcast(i32), EXPONENT,
                                             None, ALU.bitwise_and))

            def weight_scale(n):
                power(n)
                link(nc.vector.tensor_scalar(inv_w[n], pow2[:, n:n + 1], 2.0 ** -14, None, ALU.mult))
                nc.vector.reciprocal(w_scale[n], inv_w[n]).then_inc(w_scale_ready, 1)
                dve.wait_ge(w_scale_ready, n + 1)

            def split_lo(n, p):
                s = slice(p * PIECE, (p + 1) * PIECE)
                dve.wait_ge(w_hi_ready[n], p + 1)
                nc.vector.scalar_tensor_tensor(out=w_lo[n][:, s], in0=w32[n][:, s], scalar=w_scale[n],
                                               in1=w_hi[n][:, s], op0=ALU.mult,
                                               op1=ALU.subtract).then_inc(w_lo_ready[n], 1)

            def x_magnitude(n):
                dve.wait_ge(x_loaded[n], 16)
                magnitude(2, n, x_all[:, n * XM * XC:(n + 1) * XM * XC])

            def common_scales():
                dve.wait_ge(magn_ready, 2 * KC + NX)
                nc.vector.tensor_reduce(most[:, 2:3], magn[2][:, :], AX.X, ALU.max).then_inc(most_ready, 1)
                power(2)
                link(nc.vector.tensor_scalar(inv_x, pow2[:, 2:3], 2.0 ** -14, None, ALU.mult))
                link(nc.vector.tensor_tensor(s_x, inv_x, inv_w[0], ALU.mult))
                link(nc.vector.tensor_scalar(s_h, inv_w[1], 2.0 ** -15, None, ALU.mult))
                link(nc.vector.tensor_tensor(z_unscale, s_x, s_h, ALU.max))
                link(nc.vector.reciprocal(s_both, z_unscale))
                link(nc.vector.tensor_tensor(x_scale, s_both, inv_w[0], ALU.mult))
                link(nc.vector.tensor_tensor(h_scale, s_both, inv_w[1], ALU.mult))
                nc.vector.reciprocal(h_unscale, h_scale).then_inc(scales_ready, 1)
                dve.wait_ge(scales_ready, 1)

            def split_x(first_step, u):
                n = C * XC
                src = x_all[:, bass.ds(first_step * XC, n)]
                s = slice(u * XC, u * XC + n)
                nc.vector.tensor_scalar(x_hi[:, s], src, x_scale, None, ALU.mult).then_inc(xs_hi, 1)
                return src, s

            def split_x_lo(src, s, done):
                dve.wait_ge(xs_hi, done)
                nc.vector.scalar_tensor_tensor(out=x_lo[:, s], in0=src, scalar=x_scale, in1=x_hi[:, s],
                                               op0=ALU.mult, op1=ALU.subtract).then_inc(xs_lo, 1)

            def cell(t):
                dve.wait_ge(g_ready, t + 1)
                dve.wait_ge(gates_ready, t + 1)
                nc.vector.tensor_tensor(prod[:, :], ifo[:, 0:2 * HS], gc[:, :], ALU.mult).then_inc(prod_ready, 1)
                dve.wait_ge(prod_ready, t + 1)
                nc.vector.tensor_tensor(gc[:, HS:2 * HS], prod[:, 0:HS], prod[:, HS:2 * HS],
                                        ALU.add).then_inc(c_ready, 1)
                dve.wait_ge(tanhc_ready, t + 1)

            def residual(it, u, unscale):
                if u % C == 0:
                    dve.wait_ge(res_loaded[u // C], 16 * it + 16)
                    if not (isinstance(it, int) and it == 0):
                        dve.wait_ge(stored[u // C], 16 * it)
                nc.vector.scalar_tensor_tensor(out=y[:, u, :], in0=h[:, :], scalar=unscale, in1=res[:, u, :],
                                               op0=ALU.mult, op1=ALU.add).then_inc(y_ready, 1)

            def scaled_h(t, wait_for):
                nc.vector.scalar_tensor_tensor(out=h[:, :], in0=tanhc[:, :], scalar=h_scale, in1=ifo[:, 2 * HS:3 * HS],
                                               op0=ALU.mult, op1=ALU.mult).then_inc(h_ready, 1)
                dve.wait_ge(h_ready, t + 1)
                nc.vector.transpose(hT[:, :], h[:, :]).then_inc(hT_ready, 1)
                dve.wait_ge(hT_ready, t + 1)
                nc.vector.tensor_copy(hT_hi[:, :], hT[:, :]).then_inc(hi_ready, 1)
                dve.wait_ge(hi_ready, t - U + 2)
                nc.vector.tensor_tensor(hT_lo[:, :], hT[:, :], hT_hi[:, :], ALU.subtract).then_inc(lo_ready, 1)

            for n in range(2):
                w_magnitudes(n)
                weight_scale(n)
                if n == 0:
                    for p in range(NP // 2):
                        split_lo(0, p)
            for p in range(NP // 2, NP):
                split_lo(0, p)
            passes = [range(0, 6), range(6, 12), range(12, NX), range(0)]
            for u in range(U):
                cell(u)
                if u < U - 1:
                    nc.vector.tensor_tensor(h[:, :], tanhc[:, :], ifo[:, 2 * HS:3 * HS], ALU.mult).then_inc(h_ready, 1)
                    dve.wait_ge(h_ready, u + 1)
                    nc.vector.transpose(hT[:, :], h[:, :]).then_inc(hT_ready, 1)
                    residual(0, u, 1.0)
                else:
                    scaled_h(u, u)
                    residual(0, u, h_unscale)
                for n in passes[u]:
                    x_magnitude(n)
                if u == U - 2:
                    common_scales()
                    for half in range(2):
                        src, s = split_x(U + half * C, half * C)
                        split_x_lo(src, s, half + 1)

            def step(it, u, last):
                t = it * U + u
                cell(t)
                scaled_h(t, t)
                residual(it, u, h_unscale)
                if u % C == C - 1 and not last:
                    src, s = split_x(t + U - C + 1, u - C + 1)
                    split_x_lo(src, s, it * (U // C) + u // C + 1)

            with dve.Fori(1, NI - 1) as it:
                for u in range(U):
                    step(it, u, False)
            for u in range(U):
                step(NI - 1, u, True)

        @block.gpsimd
        def _(pool):
            def over_partitions(n):
                pool.wait_ge(most_ready, n + 1)
                nc.gpsimd.partition_all_reduce(most_all[:, n:n + 1], most[:, n:n + 1], P, RMAX).then_inc(all_ready, 1)

            over_partitions(0)
            over_partitions(1)
            pool.wait_ge(w_scale_ready, 2)
            half = PIECE // 2
            for p in range(2 * NP):
                if p == NP:
                    over_partitions(2)
                s = slice(p * half, (p + 1) * half)
                if p > 0:
                    pool.wait_ge(w_lo_ready[1], p)
                nc.gpsimd.tensor_scalar(w_scaled[:, :], w32[1][:, s], w_scale[1], None,
                                        ALU.mult).then_inc(w_scaled_ready, 1)
                pool.wait_ge(w_scaled_ready, p + 1)
                pool.wait_ge(w_hi_ready[1], p // 2 + 1)
                nc.gpsimd.tensor_tensor(w_lo[1][:, s], w_scaled[:, :], w_hi[1][:, s],
                                        ALU.subtract).then_inc(w_lo_ready[1], 1)


def kernel(x, cond_1024, L0_cond_Wx, L0_cond_Wh, L0_cond_b):
    import numpy as np
    import concourse.bacc as bacc
    from concourse import mybir as mb
    from concourse.bass_utils import run_bass_kernel_spmd

    x = np.asarray(x)
    B, T, D = x.shape
    NS, HS, KC, P = 4, 128, 4, 128
    wx = np.asarray(L0_cond_Wx).reshape(KC, P, 4, NS, HS).transpose(1, 0, 3, 2, 4)
    wh = np.asarray(L0_cond_Wh).reshape(NS, 4, 32, 4, NS, HS).transpose(0, 2, 1, 4, 3, 5)
    h0 = np.asarray(cond_1024).reshape(B, NS, 4, 32).transpose(1, 3, 2, 0)
    arrays = {
        "xT": x.reshape(B, T, KC, P).transpose(3, 1, 2, 0).reshape(P, T, KC * B),
        "xr": x.reshape(B, T, NS, HS).transpose(2, 0, 1, 3).reshape(P, T, HS),
        "h0T": h0.reshape(P, KC * B),
        "wx": wx.reshape(P, KC, NS * 4 * HS),
        "wh": wh.reshape(P, KC, NS * 4 * HS),
        "bias": np.asarray(L0_cond_b).reshape(4, NS, HS).transpose(1, 0, 2).reshape(NS, 4 * HS),
    }
    arrays = {f"in_{k}": np.ascontiguousarray(v) for k, v in arrays.items()}
    nc = bacc.Bacc("TRN2", target_bir_lowering=False, num_devices=1)
    args = [nc.dram_tensor(k, v.shape, mb.dt.from_np(v.dtype), kind="ExternalInput").ap() for k, v in arrays.items()]
    args.append(nc.dram_tensor("out_y", (P, T, HS), mb.dt.float32, kind="ExternalOutput").ap())
    lstm_residual_kernel(nc, *args)
    r = run_bass_kernel_spmd(nc, [arrays], core_ids=[0])
    y = np.asarray(r.results[0]["out_y"])
    return y.reshape(NS, B, T, HS).transpose(1, 2, 0, 3).reshape(B, T, NS * HS)
```

```python
import concourse.bass as bass
from concourse import mybir
from contextlib import ExitStack


def lstm_residual_kernel(nc: bass.Bass, xT: bass.AP, h0T: bass.AP, wx: bass.AP, wh: bass.AP,
                         bias: bass.AP, out: bass.AP):
    fp32 = mybir.dt.float32
    fp16 = mybir.dt.float16
    i32 = mybir.dt.int32
    ALU = mybir.AluOpType
    ACT = mybir.ActivationFunctionType
    AX = mybir.AxisListType
    RMAX = bass.bass_isa.ReduceOp.max

    P, T, XC = xT.shape
    NS, G = bias.shape
    B = P // NS
    KC = XC // B
    HS = G // 4
    C = 2
    U = 2 * C
    AHEAD = U - 1
    N32 = 8
    NI = T // U
    W = NS * G
    XM = 8
    NX = T // XM
    PIECE = 1024
    NP = KC * W // PIECE
    TINY = 2.0 ** -48
    EXPONENT = 0x7F800000

    POOL_LO = [range(0, 5), range(0, 2)]
    DVE_LO = [[p for p in range(NP) if p not in POOL_LO[n]] for n in range(2)]

    with ExitStack() as ctx:
        def sb(name, shape, dt=fp32):
            return ctx.enter_context(nc.sbuf_tensor(name, shape, dt))

        def sem(name):
            return ctx.enter_context(nc.semaphore(name))

        w32 = [sb(f"w{n}_32", [P, KC * W]) for n in "xh"]
        w_hi = [sb(f"w{n}_hi", [P, KC * W], fp16) for n in "xh"]
        w_lo = [sb(f"w{n}_lo", [P, KC * W], fp16) for n in "xh"]
        x_all = sb("x_all", [P, T * XC])
        x_hi = sb("x_hi", [P, U * XC], fp16)
        x_lo = sb("x_lo", [P, U * XC], fp16)
        zeros = x_hi
        bias_raw = sb("bias_raw", [P, G])
        y = sb("y", [P, U, XC])
        g = sb("g", [P, HS])
        ifo = sb("ifo", [P, 3 * HS])
        fc = sb("fc", [P, HS])
        ig = sb("ig", [P, HS])
        c = sb("c", [P, HS])
        cT = sb("cT", [P, KC * B])
        oT = sb("oT", [P, KC * B])
        tanhcT = sb("tanhcT", [P, KC * B])
        hT = sb("hT", [P, KC * B])
        hT_hi = sb("hT_hi", [P, KC * B], fp16)
        hT_lo = sb("hT_lo", [P, KC * B], fp16)
        magn = [sb(f"magn_{n}", [P, k]) for n, k in (("wx", KC), ("wh", KC), ("x", NX))]
        most = sb("most", [P, 3])
        most_all = sb("most_all", [P, 3])
        pow2 = sb("pow2", [P, 3])
        scl = sb("scl", [P, 12])
        w_scaled = sb("w_scaled", [P, PIECE // 2])
        warm = sb("warm", [P, 1])
        z = [ctx.enter_context(nc.psum_tensor(f"z{i}", [P, G], fp32)) for i in range(U)]

        w_scale = [scl[:, 0:1], scl[:, 1:2]]
        s_x, s_h, s_both = scl[:, 2:3], scl[:, 3:4], scl[:, 4:5]
        x_scale, h_scale, z_unscale, h_unscale = scl[:, 5:6], scl[:, 6:7], scl[:, 7:8], scl[:, 8:9]
        inv_w = [scl[:, 9:10], scl[:, 10:11]]
        inv_x = scl[:, 11:12]

        h0_loaded = sem("h0_loaded")
        bias_loaded = sem("bias_loaded")
        w_loaded = [[sem(f"w{n}_loaded{kc}") for kc in range(KC)] for n in "xh"]
        x_loaded = [sem(f"x_loaded{n}") for n in range(NX)]
        stored = [sem(f"stored{i}") for i in range(2)]
        zeros_set = sem("zeros_set")
        c_zeroed = sem("c_zeroed")
        opened = sem("opened")
        seeded = sem("seeded")
        x_done = sem("x_done")
        z_done = sem("z_done")
        if_ready = sem("if_ready")
        g_ready = sem("g_ready")
        o_ready = sem("o_ready")
        fc_ready = sem("fc_ready")
        ig_ready = sem("ig_ready")
        c_ready = sem("c_ready")
        cT_ready = sem("cT_ready")
        oT_ready = sem("oT_ready")
        tanhc_ready = sem("tanhc_ready")
        hT_ready = sem("hT_ready")
        hi_ready = sem("hi_ready")
        lo_ready = sem("lo_ready")
        y_ready = sem("y_ready")
        xs_hi = sem("xs_hi")
        xs_lo = sem("xs_lo")
        magn_ready = sem("magn_ready")
        most_ready = sem("most_ready")
        all_ready = sem("all_ready")
        scalar_done = sem("scalar_done")
        w_scale_ready = sem("w_scale_ready")
        scales_ready = sem("scales_ready")
        w_hi_ready = [sem("wx_hi_ready"), sem("wh_hi_ready")]
        w_lo_ready = [sem("wx_lo_ready"), sem("wh_lo_ready")]
        w_scaled_ready = sem("w_scaled_ready")
        pool_lo_done = sem("pool_lo_done")

        block = ctx.enter_context(nc.Block())

        @block.sync
        def _(sp):
            def load_x(n):
                sp.dma_start(x_all[:, n * XM * XC:(n + 1) * XM * XC],
                             xT[:, n * XM:(n + 1) * XM, :]).then_inc(x_loaded[n], 16)

            def store(it, half):
                sp.wait_ge(y_ready, it * U + half * C + C)
                sp.dma_start(out[:, bass.ds(it * U + half * C, C), :],
                             y[:, half * C:half * C + C, :]).then_inc(stored[half], 16)

            for j in range(NS):
                sp.dma_start(bias_raw[j * B:(j + 1) * B, :], bias[j, :].partition_broadcast(B)).then_inc(bias_loaded, 16)
            load_x(0)
            for n in range(2):
                for kc in range(KC):
                    sp.dma_start(w32[n][:, kc * W:(kc + 1) * W], (wx, wh)[n][:, kc, :]).then_inc(w_loaded[n][kc], 16)
                if n == 0:
                    sp.dma_start(hT[:, :], h0T).then_inc(h0_loaded, 16)
            for n in range(1, NX):
                load_x(n)
            with sp.Fori(1, NI) as it:
                for half in range(2):
                    store(it - 1, half)
            for half in range(2):
                store(NI - 1, half)
            for half in range(2):
                sp.wait_ge(stored[half], 16 * NI)

        @block.tensor
        def _(pe):
            def product(u, stationary, moving, cols, last, arrivals=()):
                for kc in range(KC):
                    if arrivals:
                        pe.wait_ge(arrivals[kc], 16)
                    for j in range(NS):
                        mm = pe.matmul(z[u][j * B:(j + 1) * B, :], stationary[:, cols + kc * B:cols + (kc + 1) * B],
                                       moving[:, kc * W + j * G:kc * W + (j + 1) * G], start=False,
                                       stop=last and kc == KC - 1, skip_group_check=True)
                return mm

            def x_part32(t):
                pe.wait_ge(seeded, t + 1)
                product(t % U, x_all, w32[0], t * XC, False, w_loaded[0] if t == 0 else ()).then_inc(x_done, 1)

            def h_part32(t):
                if t > 0:
                    pe.wait_ge(hT_ready, t)
                product(t % U, hT, w32[1], 0, True, w_loaded[1] if t == 0 else ()).then_inc(z_done, 1)

            def x_part(t, half, u):
                pe.wait_ge(seeded, t + 1)
                if u % C == 0:
                    pe.wait_ge(xs_lo, half - N32 // C + 1)
                product(u, x_hi, w_hi[0], u * XC, False)
                product(u, x_hi, w_lo[0], u * XC, False)
                product(u, x_lo, w_hi[0], u * XC, False).then_inc(x_done, 1)

            def h_part(t, u):
                pe.wait_ge(hi_ready, t - N32 + 1)
                product(u, hT_hi, w_hi[1], 0, False)
                product(u, hT_hi, w_lo[1], 0, False)
                pe.wait_ge(lo_ready, t - N32 + 1)
                product(u, hT_lo, w_hi[1], 0, True).then_inc(z_done, 1)

            pe.wait_ge(zeros_set, 1)
            for i in range(U):
                for j in range(NS):
                    mm = pe.matmul(z[i][j * B:(j + 1) * B, :], zeros[:, 0:B], zeros[:, :], start=True, stop=True)
                mm.then_inc(opened, 1)

            pe.wait_ge(x_loaded[0], 16)
            for t in range(AHEAD):
                x_part32(t)
            pe.wait_ge(h0_loaded, 16)
            for t in range(N32):
                h_part32(t)
                if t + AHEAD == N32:
                    pe.wait_ge(w_hi_ready[0], NP)
                    pe.wait_ge(w_lo_ready[0], len(DVE_LO[0]))
                    pe.wait_ge(pool_lo_done, 2 * len(POOL_LO[0]))
                if t + AHEAD < N32:
                    x_part32(t + AHEAD)
                else:
                    x_part(t + AHEAD, (t + AHEAD) // C, (t + AHEAD) % U)
            pe.wait_ge(w_hi_ready[1], NP)
            pe.wait_ge(w_lo_ready[1], len(DVE_LO[1]))
            pe.wait_ge(pool_lo_done, 2 * (len(POOL_LO[0]) + len(POOL_LO[1])))
            with pe.Fori(N32 // U, NI - 1) as it:
                for u in range(U):
                    h_part(it * U + u, u)
                    x_part(it * U + u + AHEAD, it * (U // C) + (u + AHEAD) // C, (u + AHEAD) % U)
            for u in range(U):
                h_part(T - U + u, u)
                if u + AHEAD < U:
                    x_part(T - U + u + AHEAD, (T - U + u + AHEAD) // C, u + AHEAD)

        @block.scalar
        def _(act):
            act.wait_ge(zeros_set, 1)
            nc.scalar.activation(warm[:, :], zeros[:, 0:1], ACT.Sigmoid)
            act.wait_ge(bias_loaded, 16 * NS)
            for i in range(U):
                act.wait_ge(opened, i + 1)
                nc.scalar.activation(z[i][:, :], bias_raw[:, :], ACT.Copy).then_inc(seeded, 1)

            def gates(t, u, unscale):
                act.wait_ge(z_done, t + 1)
                nc.scalar.activation(ifo[:, 0:2 * HS], z[u][:, 0:2 * HS], ACT.Sigmoid,
                                     scale=unscale).then_inc(if_ready, 1)
                nc.scalar.activation(g[:, :], z[u][:, 3 * HS:4 * HS], ACT.Tanh, scale=unscale).then_inc(g_ready, 1)
                nc.scalar.activation(ifo[:, 2 * HS:3 * HS], z[u][:, 2 * HS:3 * HS], ACT.Sigmoid,
                                     scale=unscale).then_inc(o_ready, 1)
                act.wait_ge(cT_ready, t + 1)
                nc.scalar.activation(tanhcT[:, :], cT[:, :], ACT.Tanh).then_inc(tanhc_ready, 1)

            def seed(u, scale):
                nc.scalar.activation(z[u][:, :], bias_raw[:, :], ACT.Copy, scale=scale).then_inc(seeded, 1)

            def split_hi(n, first, count):
                for p in range(first, first + count):
                    s = slice(p * PIECE, (p + 1) * PIECE)
                    nc.scalar.activation(w_hi[n][:, s], w32[n][:, s], ACT.Copy,
                                         scale=w_scale[n]).then_inc(w_hi_ready[n], 1)

            unscale_reg = act.alloc_register("unscale_reg")
            act.wait_ge(w_scale_ready, 1)
            split_hi(0, 0, NP)
            for t in range(N32):
                gates(t, t % U, 1.0)
                if t == N32 - U:
                    act.wait_ge(scales_ready, 1)
                    act.reg_load(unscale_reg, z_unscale[0:1, :].bitcast(i32))
                act.wait_ge(o_ready, t + 1)
                seed(t % U, 1.0 if t + U < N32 else s_both)
                if t == 0:
                    act.wait_ge(w_scale_ready, 2)
                split_hi(1, min(3 * t, NP), min(3, max(NP - 3 * t, 0)))
            with act.Fori(N32 // U, NI - 1) as it:
                for u in range(U):
                    t = it * U + u
                    gates(t, u, unscale_reg)
                    act.wait_ge(o_ready, t + 1)
                    seed(u, s_both)
            for u in range(U):
                gates(T - U + u, u, unscale_reg)

        @block.vector
        def _(dve):
            nc.vector.memset(zeros[:, :], 0.0).then_inc(zeros_set, 1)
            nc.vector.memset(c[:, :], 0.0).then_inc(c_zeroed, 1)
            dve.wait_ge(c_zeroed, 1)
            count = [0]

            def link(ins):
                count[0] += 1
                ins.then_inc(scalar_done, 1)
                dve.wait_ge(scalar_done, count[0])

            def magnitude(n, piece, src):
                nc.vector.tensor_reduce(magn[n][:, piece:piece + 1], src, AX.X, ALU.max,
                                        apply_absolute_value=True).then_inc(magn_ready, 1)

            def w_magnitudes(n):
                for kc in range(KC):
                    dve.wait_ge(w_loaded[n][kc], 16)
                    magnitude(n, kc, w32[n][:, kc * W:(kc + 1) * W])
                dve.wait_ge(magn_ready, KC * (n + 1))
                nc.vector.tensor_reduce(most[:, n:n + 1], magn[n][:, :], AX.X, ALU.max).then_inc(most_ready, 1)

            def power(n):
                dve.wait_ge(all_ready, n + 1)
                link(nc.vector.tensor_scalar(pow2[:, n:n + 1], most_all[:, n:n + 1], TINY, None, ALU.max))
                link(nc.vector.tensor_scalar(pow2[:, n:n + 1].bitcast(i32), pow2[:, n:n + 1].bitcast(i32), EXPONENT,
                                             None, ALU.bitwise_and))

            def weight_scale(n):
                power(n)
                link(nc.vector.tensor_scalar(inv_w[n], pow2[:, n:n + 1], 2.0 ** -14, None, ALU.mult))
                nc.vector.reciprocal(w_scale[n], inv_w[n]).then_inc(w_scale_ready, 1)
                dve.wait_ge(w_scale_ready, n + 1)

            def split_lo(n, p):
                s = slice(p * PIECE, (p + 1) * PIECE)
                dve.wait_ge(w_hi_ready[n], p + 1)
                nc.vector.scalar_tensor_tensor(out=w_lo[n][:, s], in0=w32[n][:, s], scalar=w_scale[n],
                                               in1=w_hi[n][:, s], op0=ALU.mult,
                                               op1=ALU.subtract).then_inc(w_lo_ready[n], 1)

            def x_magnitude(n):
                dve.wait_ge(x_loaded[n], 16)
                magnitude(2, n, x_all[:, n * XM * XC:(n + 1) * XM * XC])

            def common_scales():
                dve.wait_ge(magn_ready, 2 * KC + NX)
                nc.vector.tensor_reduce(most[:, 2:3], magn[2][:, :], AX.X, ALU.max).then_inc(most_ready, 1)
                power(2)
                link(nc.vector.tensor_scalar(inv_x, pow2[:, 2:3], 2.0 ** -14, None, ALU.mult))
                link(nc.vector.tensor_tensor(s_x, inv_x, inv_w[0], ALU.mult))
                link(nc.vector.tensor_scalar(s_h, inv_w[1], 2.0 ** -15, None, ALU.mult))
                link(nc.vector.tensor_tensor(z_unscale, s_x, s_h, ALU.max))
                link(nc.vector.reciprocal(s_both, z_unscale))
                link(nc.vector.tensor_tensor(x_scale, s_both, inv_w[0], ALU.mult))
                link(nc.vector.tensor_tensor(h_scale, s_both, inv_w[1], ALU.mult))
                nc.vector.reciprocal(h_unscale, h_scale).then_inc(scales_ready, 1)
                dve.wait_ge(scales_ready, 1)

            def split_x(half, u):
                n = C * XC
                src = x_all[:, bass.ds(half * n, n)]
                s = slice(u * XC, u * XC + n)
                nc.vector.tensor_scalar(x_hi[:, s], src, x_scale, None, ALU.mult).then_inc(xs_hi, 1)
                dve.wait_ge(xs_hi, half - N32 // C + 1)
                nc.vector.scalar_tensor_tensor(out=x_lo[:, s], in0=src, scalar=x_scale, in1=x_hi[:, s],
                                               op0=ALU.mult, op1=ALU.subtract).then_inc(xs_lo, 1)

            def cell(t):
                dve.wait_ge(if_ready, t + 1)
                nc.vector.tensor_tensor(fc[:, :], ifo[:, HS:2 * HS], c[:, :], ALU.mult).then_inc(fc_ready, 1)
                dve.wait_ge(g_ready, t + 1)
                nc.vector.tensor_tensor(ig[:, :], ifo[:, 0:HS], g[:, :], ALU.mult).then_inc(ig_ready, 1)
                dve.wait_ge(fc_ready, t + 1)
                dve.wait_ge(ig_ready, t + 1)
                nc.vector.tensor_tensor(c[:, :], fc[:, :], ig[:, :], ALU.add).then_inc(c_ready, 1)
                dve.wait_ge(c_ready, t + 1)
                nc.vector.transpose(cT[:, :], c[:, :]).then_inc(cT_ready, 1)
                dve.wait_ge(o_ready, t + 1)
                nc.vector.transpose(oT[:, :], ifo[:, 2 * HS:3 * HS]).then_inc(oT_ready, 1)
                dve.wait_ge(oT_ready, t + 1)
                dve.wait_ge(tanhc_ready, t + 1)

            def output(t, it, u, unscale):
                if u % C == 0 and not (isinstance(it, int) and it == 0):
                    dve.wait_ge(stored[u // C], 16 * it)
                dve.wait_ge(hT_ready, t + 1)
                nc.vector.scalar_tensor_tensor(out=y[:, u, :], in0=hT[:, :], scalar=unscale,
                                               in1=x_all[:, bass.ds(t * XC, XC)], op0=ALU.mult,
                                               op1=ALU.add).then_inc(y_ready, 1)

            def plain_h(t):
                nc.vector.tensor_tensor(hT[:, :], tanhcT[:, :], oT[:, :], ALU.mult).then_inc(hT_ready, 1)

            def scaled_h(t):
                nc.vector.scalar_tensor_tensor(out=hT_hi[:, :], in0=tanhcT[:, :], scalar=h_scale, in1=oT[:, :],
                                               op0=ALU.mult, op1=ALU.mult).then_inc(hi_ready, 1)
                nc.vector.scalar_tensor_tensor(out=hT[:, :], in0=tanhcT[:, :], scalar=h_scale, in1=oT[:, :],
                                               op0=ALU.mult, op1=ALU.mult).then_inc(hT_ready, 1)
                dve.wait_ge(hi_ready, t - N32 + 2)
                dve.wait_ge(hT_ready, t + 1)
                nc.vector.tensor_tensor(hT_lo[:, :], hT[:, :], hT_hi[:, :], ALU.subtract).then_inc(lo_ready, 1)

            w_magnitudes(0)
            weight_scale(0)
            w_magnitudes(1)
            passes = [range(4 * t, min(4 * t + 4, NX)) for t in range(N32)]
            for t in range(N32):
                cell(t)
                if t < N32 - 1:
                    plain_h(t)
                    output(t, t // U, t % U, 1.0)
                else:
                    scaled_h(t)
                    output(t, t // U, t % U, h_unscale)
                if t == 0:
                    weight_scale(1)
                for n in passes[t]:
                    x_magnitude(n)
                if t == N32 - U - 1:
                    common_scales()
                if t >= N32 - U and t % C == 0:
                    split_x(t // C + U // C, t % U)
                if t == N32 - U:
                    for p in DVE_LO[0]:
                        split_lo(0, p)
                elif N32 - U < t < N32 - 1:
                    for p in DVE_LO[1][t - N32 + U - 1::U - 2]:
                        split_lo(1, p)

            def step(it, u, last):
                t = it * U + u
                cell(t)
                scaled_h(t)
                output(t, it, u, h_unscale)
                if u % C == 0 and not last:
                    split_x(it * (U // C) + u // C + U // C, u)

            with dve.Fori(N32 // U, NI - 1) as it:
                for u in range(U):
                    step(it, u, False)
            for u in range(U):
                step(NI - 1, u, True)

        @block.gpsimd
        def _(pool):
            def over_partitions(n):
                pool.wait_ge(most_ready, n + 1)
                nc.gpsimd.partition_all_reduce(most_all[:, n:n + 1], most[:, n:n + 1], P, RMAX).then_inc(all_ready, 1)

            def split_lo(n, p):
                for i in range(2):
                    s = slice((2 * p + i) * PIECE // 2, (2 * p + i + 1) * PIECE // 2)
                    done[0] += 1
                    if done[0] > 1:
                        pool.wait_ge(pool_lo_done, done[0] - 1)
                    nc.gpsimd.tensor_scalar(w_scaled[:, :], w32[n][:, s], w_scale[n], None,
                                            ALU.mult).then_inc(w_scaled_ready, 1)
                    pool.wait_ge(w_scaled_ready, done[0])
                    pool.wait_ge(w_hi_ready[n], p + 1)
                    nc.gpsimd.tensor_tensor(w_lo[n][:, s], w_scaled[:, :], w_hi[n][:, s],
                                            ALU.subtract).then_inc(pool_lo_done, 1)

            done = [0]
            over_partitions(0)
            pool.wait_ge(w_scale_ready, 1)
            split_lo(0, POOL_LO[0][0])
            over_partitions(1)
            for p in POOL_LO[0][1:]:
                split_lo(0, p)
            over_partitions(2)
            pool.wait_ge(w_scale_ready, 2)
            for p in POOL_LO[1]:
                split_lo(1, p)


def kernel(x, cond_1024, L0_cond_Wx, L0_cond_Wh, L0_cond_b):
    import numpy as np
    import concourse.bacc as bacc
    from concourse import mybir as mb
    from concourse.bass_utils import run_bass_kernel_spmd

    x = np.asarray(x)
    B, T, D = x.shape
    NS, HS, KC, P = 4, 128, 4, 128
    wx, wh = (np.asarray(w).reshape(NS, KC, 32, 4, NS, HS).transpose(0, 2, 1, 4, 3, 5).reshape(P, KC, NS * 4 * HS)
              for w in (L0_cond_Wx, L0_cond_Wh))
    arrays = {
        "xT": x.reshape(B, T, NS, KC, 32).transpose(2, 4, 1, 3, 0).reshape(P, T, KC * B),
        "h0T": np.asarray(cond_1024).reshape(B, NS, KC, 32).transpose(1, 3, 2, 0).reshape(P, KC * B),
        "wx": wx,
        "wh": wh,
        "bias": np.asarray(L0_cond_b).reshape(4, NS, HS).transpose(1, 0, 2).reshape(NS, 4 * HS),
    }
    arrays = {f"in_{k}": np.ascontiguousarray(v) for k, v in arrays.items()}
    nc = bacc.Bacc("TRN2", target_bir_lowering=False, num_devices=1)
    args = [nc.dram_tensor(k, v.shape, mb.dt.from_np(v.dtype), kind="ExternalInput").ap() for k, v in arrays.items()]
    args.append(nc.dram_tensor("out_y", (P, T, KC * B), mb.dt.float32, kind="ExternalOutput").ap())
    lstm_residual_kernel(nc, *args)
    r = run_bass_kernel_spmd(nc, [arrays], core_ids=[0])
    y = np.asarray(r.results[0]["out_y"])
    return y.reshape(NS, 32, T, KC, B).transpose(4, 2, 0, 3, 1).reshape(B, T, D)
```
